# Optimizing a Trainium2 kernel written in Bass

```python
import numpy as np
import jax
import jax.numpy as jnp

def _softmax(x, axis=-1):
    return jax.nn.softmax(x, axis=axis)

def _gelu(x):
    return jax.nn.gelu(x, approximate=True)

def _silu(x):
    return jax.nn.silu(x)

def _sigmoid(x):
    return jax.nn.sigmoid(x)

def _layernorm(x, axis=-1, eps=1e-05):
    m = jnp.mean(x, axis=axis, keepdims=True)
    v = jnp.var(x, axis=axis, keepdims=True)
    return (x - m) / jnp.sqrt(v + eps)

def _scatter_add(tgt, idx, src, axis=0):
    return tgt.at[idx].add(src)

def _segment_sum(src, seg, n):
    return jax.ops.segment_sum(src, seg, n)
kernel_name = 'mk_adaln_ffn_d2_seqx_r4_892973'

def setup_inputs(seed: int=0):
    np.random.seed(seed)
    _w = jnp.asarray

    def _rec_inputs():
        import jax
        import jax.numpy as jnp
        _rk = jax.random.key(seed)
        x = -7.109e-05 + 0.9999 * jax.random.normal(jax.random.fold_in(_rk, 1), (64, 64, 1024), jnp.float32)
        _lenS = 64 - jax.random.randint(jax.random.fold_in(_rk, 7), (64,), 0, max(1, 64 // 4) + 1, jnp.int32)
        _lenS2 = 64 - jax.random.randint(jax.random.fold_in(_rk, 8), (64,), 0, max(1, 64 // 4) + 1, jnp.int32)
        itok_B_0_15 = jax.random.randint(jax.random.fold_in(_rk, 11), (64,), 0, 16, jnp.int32)
        itok_B_1_14 = jax.random.randint(jax.random.fold_in(_rk, 12), (64,), 1, 15, jnp.int32)
        return (x, itok_B_0_15, itok_B_1_14)
    x, itok_B_0_15, itok_B_1_14 = _rec_inputs()

    def _L0_cond_setup():
        import jax, jax.numpy as jnp
        import numpy as np
        B, C, T = (64, 64, 1024)
        S, D = (16, 64)
        key = jax.random.key(seed)
        k1, k2, k3 = jax.random.split(key, 3)
        x = jax.random.normal(k1, (B, C, T), dtype=jnp.float32)
        condition = jax.random.randint(k2, (B,), 0, S, dtype=jnp.int64)
        bound = float(np.sqrt(6.0 / C))
        weights = jax.random.uniform(k3, (S, C, D), dtype=jnp.float32, minval=-bound, maxval=bound)
        return {'x': x, 'condition': condition, 'weights': weights}
    _L0_cond_all = _L0_cond_setup()
    _L0_cond_in = {k: v for k, v in _L0_cond_all.items() if k in ('weights',)}
    del _L0_cond_all

    def _L0_ffn_setup():
        import jax, jax.numpy as jnp
        import numpy as np
        B_, S, D = (4, 1024, 1024)
        E, R, O = (8, 16, 1024)
        TOP_K = 2
        SCALING = 8.0 / R
        key = jax.random.key(seed)
        ks = jax.random.split(key, 5)
        x = jax.random.normal(ks[0], (B_, S, D), dtype=jnp.float32)
        router_w = jax.random.normal(ks[1], (E, D), dtype=jnp.float32) * (1.0 / np.sqrt(D))
        router_b = jax.random.normal(ks[2], (E,), dtype=jnp.float32) * 0.01
        A = jax.random.normal(ks[3], (E, R, D), dtype=jnp.float32) * (1.0 / np.sqrt(D))
        Bm = jax.random.normal(ks[4], (E, O, R), dtype=jnp.float32) * 0.02
        return {'x': x, 'router_w': router_w, 'router_b': router_b, 'A': A, 'Bm': Bm}
    _L0_ffn_all = _L0_ffn_setup()
    _L0_ffn_in = {k: v for k, v in _L0_ffn_all.items() if k in ('router_w', 'router_b', 'A', 'Bm')}
    del _L0_ffn_all

    def _L1_cond_setup():
        import jax, jax.numpy as jnp
        import numpy as np
        B, S, D_IN = (8, 512, 1024)
        A, D_OUT = (16, 1024)
        key = jax.random.key(seed)
        k1, k2, k3 = jax.random.split(key, 3)
        x = jax.random.normal(k1, (B, S, D_IN), dtype=jnp.float32)
        weight = jax.random.normal(k2, (A, D_OUT, D_IN), dtype=jnp.float32) * 0.02
        adapter_ids = jax.random.randint(k3, (B,), 0, A, dtype=jnp.int64)
        return {'x': x, 'weight': weight, 'adapter_ids': adapter_ids}
    _L1_cond_all = _L1_cond_setup()
    _L1_cond_in = {k: v for k, v in _L1_cond_all.items() if k in ('weight',)}
    del _L1_cond_all

    def _L1_ffn_setup():
        import jax, jax.numpy as jnp
        import numpy as np
        TOP_K = 2
        SCALING = 32.0 / 64.0
        key = jax.random.key(seed)
        ks = jax.random.split(key, 6)
        Bsz, S, Din, Dout, R, E = (4, 512, 1024, 1024, 64, 16)
        x = jax.random.normal(ks[0], (Bsz, S, Din), dtype=jnp.float32)
        base_w = jax.random.normal(ks[1], (Dout, Din), dtype=jnp.float32) * 0.02
        base_b = jax.random.normal(ks[2], (Dout,), dtype=jnp.float32) * 0.02
        A = jax.random.normal(ks[3], (R, Din), dtype=jnp.float32) * (1.0 / np.sqrt(Din))
        B = jax.random.normal(ks[4], (E, Dout, R), dtype=jnp.float32) * 0.02
        router_w = jax.random.normal(ks[5], (E, Din), dtype=jnp.float32) * 0.02
        return {'x': x, 'base_w': base_w, 'base_b': base_b, 'A': A, 'B': B, 'router_w': router_w}
    _L1_ffn_all = _L1_ffn_setup()
    _L1_ffn_in = {k: v for k, v in _L1_ffn_all.items() if k in ('base_w', 'base_b', 'A', 'B', 'router_w')}
    del _L1_ffn_all
    return {'x': x, 'itok_B_0_15': itok_B_0_15, 'itok_B_1_14': itok_B_1_14, 'L0_cond_weights': _L0_cond_in['weights'], 'L0_ffn_router_w': _L0_ffn_in['router_w'], 'L0_ffn_router_b': _L0_ffn_in['router_b'], 'L0_ffn_A': _L0_ffn_in['A'], 'L0_ffn_Bm': _L0_ffn_in['Bm'], 'L1_cond_weight': _L1_cond_in['weight'], 'L1_ffn_base_w': _L1_ffn_in['base_w'], 'L1_ffn_base_b': _L1_ffn_in['base_b'], 'L1_ffn_A': _L1_ffn_in['A'], 'L1_ffn_B': _L1_ffn_in['B'], 'L1_ffn_router_w': _L1_ffn_in['router_w']}

def reference(x, itok_B_0_15, itok_B_1_14, L0_cond_weights, L0_ffn_router_w, L0_ffn_router_b, L0_ffn_A, L0_ffn_Bm, L1_cond_weight, L1_ffn_base_w, L1_ffn_base_b, L1_ffn_A, L1_ffn_B, L1_ffn_router_w):
    import jax
    import jax.numpy as jnp

    def _L0_cond_ref(x, condition, weights):
        import jax, jax.numpy as jnp
        import numpy as np
        B, C, T = (64, 64, 1024)
        S, D = (16, 64)
        W = weights[condition]
        return jnp.einsum('bct,bcd->bdt', x, W)

    def _L0_ffn_ref(x, router_w, router_b, A, Bm):
        import jax, jax.numpy as jnp
        import numpy as np
        B_, S, D = (4, 1024, 1024)
        E, R, O = (8, 16, 1024)
        TOP_K = 2
        SCALING = 8.0 / R
        flat = x.reshape(-1, x.shape[-1])
        N = flat.shape[0]
        logits = flat @ router_w.T + router_b
        probs = jax.nn.softmax(logits, axis=-1)
        topv, topi = jax.lax.top_k(probs, TOP_K)
        gates = topv / jnp.sum(topv, axis=-1, keepdims=True)
        w = jnp.zeros((N, E), dtype=flat.dtype).at[jnp.arange(N)[:, None], topi].add(gates)
        h = jnp.einsum('nd,erd->ner', flat, A)
        hw = h * w[:, :, None]
        out = jnp.einsum('ner,eor->no', hw, Bm) * SCALING
        return out.reshape(*x.shape[:-1], O)

    def _L1_cond_ref(x, weight, adapter_ids):
        import jax, jax.numpy as jnp
        import numpy as np
        B, S, D_IN = (8, 512, 1024)
        A, D_OUT = (16, 1024)
        w = weight[adapter_ids]
        return jnp.einsum('bij,bkj->bik', x, w)

    def _L1_ffn_ref(x, base_w, base_b, A, B, router_w):
        import jax, jax.numpy as jnp
        import numpy as np
        TOP_K = 2
        SCALING = 32.0 / 64.0
        base_out = jnp.einsum('bsi,oi->bso', x, base_w) + base_b
        res_hidden = jnp.einsum('bsi,ri->bsr', x, A)
        logits = jnp.einsum('bsi,ei->bse', x, router_w)
        probs = jax.nn.softmax(logits, axis=-1)
        topw, topi = jax.lax.top_k(probs, TOP_K)
        topw = topw / (jnp.sum(topw, axis=-1, keepdims=True) + 1e-06)
        num_experts = B.shape[0]
        combine = jnp.sum(jax.nn.one_hot(topi, num_experts, dtype=x.dtype) * topw[..., None], axis=-2)
        delta = jnp.einsum('bse,bsr,eor->bso', combine, res_hidden, B)
        return base_out + delta * SCALING
    x = x + _L0_ffn_ref(_L0_cond_ref(x, itok_B_0_15, L0_cond_weights), L0_ffn_router_w, L0_ffn_router_b, L0_ffn_A, L0_ffn_Bm)
    x = x + _L1_ffn_ref(_L1_cond_ref(x, L1_cond_weight, itok_B_1_14), L1_ffn_base_w, L1_ffn_base_b, L1_ffn_A, L1_ffn_B, L1_ffn_router_w)
    return x

_drawn_inputs = setup_inputs


def setup_inputs(seed=0):
    import zlib

    import numpy as np

    out = dict(_drawn_inputs(seed))
    spreads = {}
    factors = {'L0_ffn_router_b': 64.0, 'L1_ffn_base_b': 3.013}
    for name, (base, spread) in spreads.items():
        noise = np.random.default_rng([zlib.crc32(name.encode()), seed]).standard_normal(out[name].shape)
        drawn = base * np.exp(spread * noise) if base else spread * noise
        out[name] = jnp.asarray(drawn.astype(out[name].dtype))
    for name, factor in factors.items():
        out[name] = (out[name] * factor).astype(out[name].dtype)
    return out
```

```python
from contextlib import ExitStack

import concourse.bass as bass
from concourse import mybir


F32 = mybir.dt.float32
F32R = mybir.dt.float32r
I32 = mybir.dt.int32
ALU = mybir.AluOpType
ACT = mybir.ActivationFunctionType
AX = mybir.AxisListType

P = 128
NB, C, D = 64, 64, 1024
KC = D // P
NW = 16
E0, R0 = 8, 16
E1, R1 = 16, 64
Z0 = E0 + E0 * R0
Z1 = R1 + E1
GB = 4
GR = GB * C
GT = GR // P
NG = NB // GB
RING = 4
PAIRS_MAX = (NB + NW) // 2
SLOTS = 2 * PAIRS_MAX + 16
DUMMY = NB
BIG = 3.0e38

T_LOAD, T_STORE, T_ADAPTER = 0, SLOTS, 2 * SLOTS
T_START = T_ADAPTER + NW + 1
T_USED = T_START + NW + 2
T_LAST = T_USED + 1
T_END = T_LAST + NW + 1


class Chain:

    def __init__(self, engine, sem, value=0):
        self.engine, self.sem, self.value = engine, sem, value

    def __call__(self, instruction):
        instruction.then_inc(self.sem, 1)
        self.value = self.value + 1
        self.engine.wait_ge(self.sem, self.value)


def bcast(ap, axis, n):
    shape = list(ap.shape)
    shape.insert(axis, n)
    return ap.unsqueeze(axis).broadcast_to(shape)


def build(nc, xT, id0, id1, w0, p0T, rb0, b0T, w1T, baseT, q1T, bias1, out):
    x1s = nc.dram_tensor("x1_scratch", (NB, P, KC * C), F32, kind="Internal").ap()
    y1s = nc.dram_tensor("y1_scratch", (DUMMY + SLOTS, C, D), F32, kind="Internal").ap()

    ctx = ExitStack()
    with ctx:
        def sem(name):
            return ctx.enter_context(nc.semaphore(name))

        def sb(stack, name, shape, dt=F32):
            return stack.enter_context(nc.sbuf_tensor(name, shape, dt))

        w_hi = sb(ctx, "w_hi", [P, KC, D], F32R)
        w_lo = sb(ctx, "w_lo", [P, KC, D], F32R)
        consts = ctx
        ident = sb(consts, "ident", [P, P])
        table = sb(consts, "table", [1, T_END], I32)
        ids0 = sb(consts, "ids0", [1, NB], I32)
        bias = sb(consts, "bias", [P, KC])
        q_hi = sb(consts, "q_hi", [P, KC, Z1], F32R)
        q_lo = sb(consts, "q_lo", [P, KC, Z1], F32R)
        sel = sb(consts, "sel", [2 * E1, KC, P], F32R)
        desc0 = sb(consts, "desc0", [P, GT, E0])
        desc1 = sb(consts, "desc1", [P, GT, E1])
        rbias = sb(consts, "rbias", [P, E0])
        sm = sb(consts, "sm", [P, 10, GT, E1])
        sv = sb(consts, "sv", [P, 8, GT])

        with ExitStack() as s:
            xg = [sb(s, f"xg{i}", [P, KC, GR]) for i in range(RING)]
            x1g = [sb(s, "x1g0", [P, GB, KC, C])]
            p0 = sb(s, "p0", [P, KC, Z0])
            w0tab = sb(s, "w0tab", [P, NW * C])
            w0blk = [sb(s, f"w0blk{i}", [P, GT, P]) for i in range(2)]
            zsb = sb(s, "zsb", [P, GT, Z0])
            hw0 = sb(s, "hw0", [P, GT, E0 * R0])
            b0raw = sb(s, "b0raw", [P, D])
            q1raw = sb(s, "q1raw", [P, KC, Z1])
            idx = sb(s, "idx", [P, 1152])
        base_hi = sb(ctx, "base_hi", [P, KC, D], F32R)
        base_lo = sb(ctx, "base_lo", [P, KC, D], F32R)
        with ExitStack() as s:
            raw = sb(s, "raw", [P, KC, D])
            b0_hi = sb(s, "b0_hi", [P, D], F32R)
            b0_lo = sb(s, "b0_lo", [P, D], F32R)
            h0_hi = sb(s, "h0_hi", [P, GR], F32R)
            h0_lo = sb(s, "h0_lo", [P, GR], F32R)
            with ExitStack() as s0:
                x1g.append(sb(s0, "x1g1", [P, GB, KC, C]))
            xp = sb(s, "xp", [P, 2, 2, KC, C])
            xp_hi = sb(s, "xp_hi", [P, KC, P], F32R)
            xp_lo = sb(s, "xp_lo", [P, KC, P], F32R)
            yp = sb(s, "yp", [P, D])
        with ExitStack() as s:
            yn = sb(s, "yn", [P, GT, D])
            xr = sb(s, "xr", [P, GB, KC, C])
            y_hi = sb(s, "y_hi", [P, KC, GR], F32R)
            y_lo = sb(s, "y_lo", [P, KC, GR], F32R)
            hw_hi = sb(s, "hw_hi", [P, KC, GR], F32R)
            hw_lo = sb(s, "hw_lo", [P, KC, GR], F32R)
            rh2 = sb(s, "rh2", [P, GR])
            lgT = sb(s, "lgT", [E1, GR])
            comb_r = sb(s, "comb_r", [P, GT, E1], F32R)
            comb = sb(s, "comb", [P, GT, 2 * E1])
            combT = sb(s, "combT", [2 * E1, GR], F32R)
            hwt = [sb(s, f"hwt{i}", [P, GR]) for i in range(2)]

        psum = ctx.enter_context(nc.psum_tensor("psum", [P, 8 * 512], F32))

        def bank(i, n=1):
            return psum[:, i * 512:(i + n) * 512]

        z_ps = bank(0)[:, 0:GT * Z0].rearrange("p (m z) -> p m z", m=GT)
        yz_ps = bank(1)[:, 0:GT * Z0].rearrange("p (m z) -> p m z", m=GT)
        h0T_ps = bank(2)[:, 0:GR]

        const_in = sem("const_in")
        raw_in = [sem(f"raw_in{i}") for i in range(KC)]
        xg_in = [sem(f"xg_in{i}") for i in range(RING)]
        x1_out = [sem(f"x1_out{i}") for i in range(2)]
        iota_done = sem("iota_done")
        sel_done = sem("sel_done")
        ident_done = sem("ident_done")
        index_chain = sem("index_chain")
        gate_chain = sem("gate_chain")
        p0_in = sem("p0_in")
        idx_dve = sem("idx_dve")
        idx_pe = sem("idx_pe")
        table_ready = sem("table_ready")
        const_split_hi = sem("const_split_hi")
        const_split = sem("const_split")
        blk_zero = sem("blk_zero")
        blk_ready = sem("blk_ready")
        z_done = sem("z_done")
        z_copied = sem("z_copied")
        yz_done = sem("yz_done")
        shift0 = sem("shift0")
        exp0 = sem("exp0")
        hw0_ready = sem("hw0_ready")
        h0T_done = sem("h0T_done")
        h0_hi_done = sem("h0_hi_done")
        h0_lo_done = sem("h0_lo_done")
        o_done = sem("o_done")
        x1_added = sem("x1_added")
        w_hi_done = sem("w_hi_done")
        w_lo_done = sem("w_lo_done")
        base_hi_done = sem("base_hi_done")
        base_lo_done = sem("base_lo_done")
        xp_in = sem("xp_in")
        xp_hi_done = sem("xp_hi_done")
        xp_lo_done = sem("xp_lo_done")
        mm_done = sem("mm_done")
        yp_act = sem("yp_act")
        yp_dve = sem("yp_dve")
        yp_out = sem("yp_out")
        yn_in = sem("yn_in")
        xr_in = sem("xr_in")
        yT_done = sem("yT_done")
        y_hi_done = sem("y_hi_done")
        y_lo_done = sem("y_lo_done")
        base_done = sem("base_done")
        rh_done = sem("rh_done")
        rh_copied = sem("rh_copied")
        lt_done = sem("lt_done")
        shift1 = sem("shift1")
        exp1 = sem("exp1")
        comb_ready = sem("comb_ready")
        ct_done = sem("ct_done")
        combT_ready = sem("combT_ready")
        bc_done = sem("bc_done")
        hwt_ready = sem("hwt_ready")
        hw_hi_done = sem("hw_hi_done")
        hw_lo_done = sem("hw_lo_done")
        acc_done = sem("acc_done")
        out_added = sem("out_added")
        out_stored = sem("out_stored")

        iota_f = idx[:, 0:96]
        part_f = idx[:, 96:97]
        id_f = idx[0:NB, 97:98]
        q_f = idx[0:NB, 98:99]
        even_f = idx[0:NB, 99:100]
        first_f = idx[0:NB, 100:101]
        slot_f = idx[0:NB, 101:102]
        pos_b = idx[0:NB, 102:103]
        np_f = idx[0:NW, 103:104]
        used_f = idx[0:NW, 104:105]
        rank_f = idx[0:NW, 105:106]
        pos_f = idx[0:NW, 106:107]
        part16_f = idx[0:NW, 107:108]
        count_f = idx[0:NW, 108:109]
        ones_f = idx[0:NB, 128:192]
        hot_f = idx[0:NB, 192:208]
        hot_even_f = idx[0:NB, 208:224]
        tmp_f = idx[0:NB, 224:288]
        before_f = idx[0:NB, 288:352]
        m_f = idx[0:NB, 352:352 + SLOTS]
        r_f = idx[0:NW, 448:448 + NW + 1]
        g_f = idx[0:NW, 480:480 + NW + 2]
        rows_f = idx[0:1, 512:512 + T_END]
        slot_iota = idx[0:1, 760:760 + SLOTS]
        cmp_f = idx[0:NW, 760:776]
        eq_f = idx[0:NW, 776:792]
        iota_i = idx[:, 860:956].bitcast(I32)
        part_i = idx[:, 956:957].bitcast(I32)
        id_i = idx[0:NB, 957:958].bitcast(I32)
        id_row_i = idx[0:NW, 960:1024].bitcast(I32)
        hotT_f = idx[0:NW, 1024:1088]
        npw_f = idx[0:NW, 1088:1152]
        prefix_ps = bank(7)[0:NB, 0:16]
        npb_ps = bank(7)[0:NB, 16:32]
        npc_ps = bank(7)[0:NW, 32:33]
        pos_ps = bank(7)[0:NB, 33:34]
        start_ps = bank(7)[0:NB, 34:34 + NW + 2]
        rows_ps = bank(7)[0:1, 64:64 + T_LAST]
        fill_ps = bank(7)[0:1, 320:320 + SLOTS]

        block = ctx.enter_context(nc.Block())

        def w_used(e):
            return e.value_load(table[0:1, T_USED:T_USED + 1], min_val=1, max_val=NW)

        def start_of(e, u):
            return e.value_load(table[0:1, bass.ds(T_START + u, 1)], min_val=0, max_val=PAIRS_MAX)

        def xp_of(j, ks):
            return xp[:, bass.ds(j % 2, 1), :, ks, :].rearrange("p a b i c -> p (a b) i c")

        def last_of(e, u):
            return e.value_load(table[0:1, bass.ds(T_LAST + u, 1)], min_val=0, max_val=PAIRS_MAX - 1)

        @block.sync
        def _(sp):
            def load_x(g, slot):
                sp.dma_start(xg[slot][:, :, :], xT[bass.ds(g, 1), :, :, :].rearrange("g p i r -> p (g i) r")
                             ).then_inc(xg_in[slot], 16)

            sp.dma_start(p0[:, :, :], p0T).then_inc(p0_in, 16)
            for g in range(RING):
                load_x(g, g)

            def store_x(g, slot):
                sp.wait_ge(x1_added, 4 * g + 4)
                sp.dma_start(x1s[bass.ds(g * GB, GB), :, :].rearrange("b p (i c) -> p b i c", c=C),
                             x1g[slot % 2][:, :, :, :]).then_inc(x1_out[slot % 2], 16)

            with sp.Fori(0, NG // RING - 1) as t:
                g0 = t * RING
                for s in range(RING):
                    store_x(g0 + s, s)
                    load_x(g0 + s + RING, s)
            for s in range(RING):
                store_x(NG - RING + s, s)

            for s in range(2):
                sp.wait_ge(x1_out[s], 16 + 16 * (NG // 2))

            sp.wait_ge(table_ready, 1)

            def load_pair(j):
                for h in range(2):
                    b = sp.value_load(table[0:1, bass.ds(T_LOAD + 2 * j + h, 1)], min_val=0, max_val=NB - 1)
                    sp.dma_start(xp[:, bass.ds(j % 2, 1), h, :, :].rearrange("p a i c -> p (a i) c"),
                                   x1s[bass.ds(b, 1), :, :].rearrange("b p (i c) -> p (b i) c", c=C)
                                   ).then_inc(xp_in, 16)

            load_pair(0)
            sp.wait_ge(xp_in, 32)
            load_pair(1)
            used = w_used(sp)
            total = start_of(sp, used)
            with sp.Fori(0, total) as j:
                sp.wait_ge(xp_lo_done, 2 * j + 2)
                sp.wait_ge(xp_in, (j + 2) * 32)
                load_pair(j + 2)
                sp.wait_ge(yp_act, j + 1)
                sp.wait_ge(yp_dve, j + 1)
                for h in range(2):
                    b = sp.value_load(table[0:1, bass.ds(T_STORE + 2 * j + h, 1)],
                                        min_val=0, max_val=DUMMY + SLOTS - 1)
                    sp.dma_start(y1s[bass.ds(b, 1), :, :].rearrange("b c k -> (b c) k"),
                                   yp[h * C:(h + 1) * C, :]).then_inc(yp_out, 16)

            sp.wait_ge(yp_out, total * 32 + 32)
            sp.wait_ge(w_lo_done, used * KC + KC)
            sp.wait_ge(xp_lo_done, total * 2 + 2)
            sp.wait_ge(xp_in, (total + 2) * 32)

            def load_group(g):
                sp.dma_start(yn[:, :, :], y1s[bass.ds(g * GB, GB), :, :].rearrange("(m b) c k -> (b c) m k", m=GT)
                             ).then_inc(yn_in, 16)

            def load_xr(g):
                sp.dma_start(xr[:, :, :, :], x1s[bass.ds(g * GB, GB), :, :].rearrange("b p (i c) -> p b i c", c=C)
                             ).then_inc(xr_in, 16)

            def store_out(g):
                sp.wait_ge(out_added, (g + 1) * KC)
                sp.dma_start(out[bass.ds(g * GB, GB), :, :].rearrange("b p (i c) -> p b i c", c=C),
                             xr[:, :, :, :]).then_inc(out_stored, 16)
                sp.wait_ge(out_stored, (g + 1) * 16)

            load_group(0)
            load_xr(0)
            with sp.Fori(0, NG - 1) as g:
                sp.wait_ge(yT_done, (g + 1) * 4)
                load_group(g + 1)
                store_out(g)
                load_xr(g + 1)
            store_out(NG - 1)

        @block.gpsimd
        def _(pool):
            pool.iota(iota_i, pattern=[[1, 96]], base=0, channel_multiplier=0).then_inc(iota_done, 1)
            pool.iota(part_i, pattern=[[0, 1]], base=0, channel_multiplier=1).then_inc(iota_done, 1)
            pool.memset(yp[0:1, 0:1], 0.0).then_inc(yp_out, 32)
            for s in range(2):
                pool.memset(x1g[s][0:1, 0, 0, 0:1], 0.0).then_inc(x1_out[s], 16)
            pool.memset(ident[:, :], 0.0).then_inc(ident_done, 1)
            pool.wait_ge(ident_done, 1)
            pool.affine_select(out=ident[:, :], in_=ident[:, :], compare_op=ALU.not_equal, fill=1.0,
                               base=0, pattern=[[-1, P]], channel_multiplier=1).then_inc(ident_done, 1)
            for s in range(2):
                pool.memset(w0blk[s][:, :, :], 0.0).then_inc(blk_zero, 1)
            pool.wait_ge(blk_zero, 2)
            pool.wait_ge(const_in, 16 * 9)

            def w0_block(g, slot):
                for m in range(GT):
                    for h in range(2):
                        a = pool.value_load(ids0[0:1, bass.ds(g * GB + m * 2 + h, 1)], min_val=0, max_val=NW - 1)
                        last = pool.tensor_copy(w0blk[slot][h * C:(h + 1) * C, m, h * C:(h + 1) * C],
                                                w0tab[h * C:(h + 1) * C, bass.ds(a * C, C)])
                        last.then_inc(blk_ready, 1)

            def w0_blocks(t):
                for s in range(2):
                    pool.wait_ge(yz_done, 2 * t + s - 1)
                    w0_block(2 * t + s, s)

            for g in range(2):
                w0_block(g, g)
            for t in range(1, RING // 2 + 1):
                w0_blocks(t)
            pool.wait_ge(table_ready, 1)
            a0 = pool.value_load(table[0:1, T_ADAPTER:T_ADAPTER + 1], min_val=0, max_val=NW)
            for i in range(KC):
                pool.dma_start(raw[:, i, :], w1T[bass.ds(a0, 1), i, :, :].rearrange("a p k -> p (a k)")
                             ).then_inc(raw_in[i], 16)
            with pool.Fori(RING // 2 + 1, NG // 2) as t:
                w0_blocks(t)

            pool.wait_ge(blk_ready, 4 * NG)
            for i in range(KC):
                pool.wait_ge(w_hi_done, i + 1)
                pool.tensor_tensor(w_lo[:, i, :], raw[:, i, :], w_hi[:, i, :].bitcast(F32), ALU.subtract
                                   ).then_inc(w_lo_done, 1)
                pool.wait_ge(w_lo_done, i + 1)
                pool.dma_start(raw[:, i, :], baseT[i, :, :]).then_inc(raw_in[i], 16)
            used = w_used(pool)
            with pool.Fori(1, used + 1) as u:
                a = pool.value_load(table[0:1, bass.ds(T_ADAPTER + u, 1)], min_val=0, max_val=NW)
                for i in range(KC):
                    pool.wait_ge(base_lo_done, i + 1)
                    pool.wait_ge(w_lo_done, u * KC - KC + i + 1)
                    pool.dma_start(raw[:, i, :], w1T[bass.ds(a, 1), i, :, :].rearrange("a p k -> p (a k)")
                                 ).then_inc(raw_in[i], 16)

        @block.scalar
        def _(act):
            act.dma_start(id_i, id1.rearrange("(b a) -> b a", a=1)).then_inc(const_in, 16)
            act.dma_start(id_row_i, id1.partition_broadcast(NW)).then_inc(const_in, 16)
            act.dma_start(ids0[0:1, :], id0.rearrange("(a b) -> a b", a=1)).then_inc(const_in, 16)
            for h in range(2):
                act.dma_start(w0tab[h * C:(h + 1) * C, :], w0).then_inc(const_in, 16)
            act.dma_start(rbias[:, :], rb0.partition_broadcast(P)).then_inc(const_in, 16)
            act.dma_start(b0raw[:, :], b0T).then_inc(const_in, 16)
            act.dma_start(q1raw[:, :, :], q1T).then_inc(const_in, 16)
            act.dma_start(bias[:, :], bias1).then_inc(const_in, 16)

            def w_high(i, n_in):
                act.wait_ge(raw_in[i], n_in)
                act.activation(w_hi[:, i, :], raw[:, i, :], ACT.Copy).then_inc(w_hi_done, 1)

            def z_copy(g):
                act.wait_ge(z_done, g + 1)
                act.activation(zsb[:, :, :], z_ps, ACT.Copy).then_inc(z_copied, 1)

            def group0(g, last=False):
                act.wait_ge(shift0, g + 1)
                act.activation(sm[:, 1, :, 0:E0], sm[:, 0, :, 0:E0], ACT.Exp).then_inc(exp0, 1)
                if not last:
                    z_copy(g + 1)
                act.wait_ge(h0T_done, g + 1)
                act.activation(h0_hi[:, :], h0T_ps, ACT.Copy).then_inc(h0_hi_done, 1)

            z_copy(0)
            act.wait_ge(const_in, 16 * 9)
            act.activation(b0_hi[:, :], b0raw[:, :], ACT.Copy).then_inc(const_split_hi, 1)
            act.activation(q_hi[:, :, :], q1raw[:, :, :], ACT.Copy).then_inc(const_split_hi, 1)
            with act.Fori(0, NG - RING) as g:
                group0(g)
            for s in range(RING):
                for i in (2 * s, 2 * s + 1):
                    w_high(i, 16)
                group0(NG - RING + s, last=s == RING - 1)

            def x_high(j, half):
                ks = slice(half * KC // 2, (half + 1) * KC // 2)
                act.wait_ge(xp_in, 32 * j + 32)
                act.activation(xp_hi[:, ks, :].rearrange("p i (b c) -> p b i c", b=2), xp_of(j, ks),
                               ACT.Copy).then_inc(xp_hi_done, 1)

            def step(j, u_next=None):
                for i in range(KC):
                    act.wait_ge(mm_done, KC * j + i + 1)
                    if u_next is not None:
                        act.wait_ge(raw_in[i], 16 * u_next + 32)
                        act.activation(w_hi[:, i, :], raw[:, i, :], ACT.Copy).then_inc(w_hi_done, 1)
                    if i == KC // 2 - 1:
                        x_high(j + 1, 0)
                x_high(j + 1, 1)
                act.wait_ge(yp_out, 32 * j + 32)
                act.activation(yp[:, 0:512], psum[:, bass.ds(((j % 2) * 2 + 3) * 512, 512)],
                               ACT.Copy).then_inc(yp_act, 1)

            x_high(0, 0)
            x_high(0, 1)
            for s in range(2):
                act.wait_ge(x1_out[s], 16 + 16 * (NG // 2))
            for i in range(KC):
                act.wait_ge(raw_in[i], 32)
                act.activation(base_hi[:, i, :], raw[:, i, :], ACT.Copy).then_inc(base_hi_done, 1)
            act.wait_ge(table_ready, 1)
            used = w_used(act)
            with act.Fori(0, used) as u:
                first = start_of(act, u)
                last = last_of(act, u)
                with act.If(last > first):
                    with act.Fori(first, last) as j:
                        step(j)
                with act.Else():
                    act.nop()
                step(last, u + 1)

            def y_high(g):
                for q in range(4):
                    act.wait_ge(yT_done, 4 * g + q + 1)
                    act.activation(y_hi[:, 2 * q:2 * q + 2, :], bank(4 + q % 2).rearrange("p (i r) -> p i r", i=2),
                                   ACT.Copy).then_inc(y_hi_done, 1)

            def rh_copy(g):
                act.wait_ge(rh_done, g + 1)
                act.activation(lgT[:, :], bank(6)[R1:Z1, 0:GR], ACT.Copy).then_inc(rh_copied, 1)
                for h in range(2):
                    act.activation(rh2[h * R1:(h + 1) * R1, :], bank(6)[0:R1, 0:GR], ACT.Copy
                                   ).then_inc(rh_copied, 1)

            def group1(g):
                act.wait_ge(shift1, g + 1)
                act.activation(sm[:, 1, :, :], sm[:, 0, :, :], ACT.Exp).then_inc(exp1, 1)
                act.wait_ge(ct_done, g + 1)
                act.activation(combT[:, :], bank(7)[0:2 * E1, 0:GR], ACT.Copy).then_inc(combT_ready, 1)
                for j in range(KC):
                    act.wait_ge(hwt_ready, KC * g + j + 1)
                    act.activation(hw_hi[:, j, :], hwt[j % 2][:, :], ACT.Copy).then_inc(hw_hi_done, 1)

            act.wait_ge(w_lo_done, used * KC + KC)
            y_high(0)
            rh_copy(0)
            with act.Fori(0, NG - 1) as g:
                group1(g)
                act.wait_ge(base_done, g + 1)
                y_high(g + 1)
                rh_copy(g + 1)
            group1(NG - 1)

        @block.vector
        def _(dve):
            link = Chain(dve, index_chain)
            tt, ts = dve.tensor_tensor, dve.tensor_scalar

            def index_0():
                link(dve.memset(ones_f, 1.0))
                dve.wait_ge(const_in, 16 * 9)
                dve.wait_ge(iota_done, 2)
                link(dve.tensor_copy(iota_f, iota_i))
                link(dve.tensor_copy(part_f, part_i))
                link(dve.tensor_copy(id_f, id_i))
                link(dve.tensor_copy(hotT_f, id_row_i))
                link(ts(hotT_f, hotT_f, part_f[0:NW, :], None, ALU.is_equal))
                link(ts(hot_f, iota_f[0:NB, 0:NW], id_f, None, ALU.is_equal))
                ts(before_f, iota_f[0:NB, 0:NB], part_f[0:NB, :], None, ALU.is_gt).then_inc(idx_dve, 1)

            def index_1():
                dve.wait_ge(idx_pe, 1)
                link(tt(tmp_f[:, 0:NW], prefix_ps, hot_f, ALU.mult))
                link(dve.reduce_sum(q_f, tmp_f[:, 0:NW], AX.X))
                link(ts(tmp_f[:, 0:NB // 2], iota_f[0:NB, 0:NB:2], q_f, None, ALU.is_equal))
                link(dve.reduce_sum(even_f, tmp_f[:, 0:NB // 2], AX.X))
                ts(hot_even_f, hot_f, even_f, None, ALU.mult).then_inc(idx_dve, 1)

            def index_2():
                dve.wait_ge(idx_pe, 2)
                link(dve.tensor_copy(np_f, npc_ps))
                link(ts(cmp_f, npb_ps[0:NW, :], 0.0, None, ALU.is_gt))
                link(dve.reduce_sum(count_f, cmp_f, AX.X))
                link(ts(used_f, np_f, 0.0, None, ALU.is_gt))
                link(ts(cmp_f, npb_ps[0:NW, :], np_f, None, ALU.is_gt))
                link(ts(eq_f, npb_ps[0:NW, :], np_f, None, ALU.is_equal))
                link(ts(tmp_f[0:NW, 0:NW], iota_f[0:NW, 0:NW], part_f[0:NW, :], None, ALU.is_lt))
                link(tt(eq_f, eq_f, tmp_f[0:NW, 0:NW], ALU.mult))
                link(tt(cmp_f, cmp_f, eq_f, ALU.add))
                link(dve.reduce_sum(rank_f, cmp_f, AX.X))
                link(tt(pos_f, count_f, rank_f, ALU.subtract))
                link(ts(pos_f, pos_f, 2.0, -1.0, ALU.mult, ALU.add))
                link(ts(rank_f, rank_f, 2.0, None, ALU.mult))
                link(tt(pos_f, pos_f, rank_f, ALU.min))
                link(ts(r_f, iota_f[0:NW, 0:NW + 1], pos_f, None, ALU.is_equal))
                link(ts(r_f, r_f, used_f, None, ALU.mult))
                link(ts(npw_f, ones_f[0:NW, :], np_f, None, ALU.mult))
                link(ts(part16_f, part_f[0:NW, :], float(NW), None, ALU.subtract))
                ts(g_f, iota_f[0:NW, 0:NW + 2], pos_f, None, ALU.is_gt).then_inc(idx_dve, 1)

            def index_3():
                dve.wait_ge(idx_pe, 3)
                link(dve.tensor_copy(pos_b, pos_ps))
                link(ts(tmp_f[:, 0:NW + 2], iota_f[0:NB, 0:NW + 2], pos_b, None, ALU.is_equal))
                link(tt(tmp_f[:, 0:NW + 2], start_ps, tmp_f[:, 0:NW + 2], ALU.mult))
                link(dve.reduce_sum(first_f, tmp_f[:, 0:NW + 2], AX.X))
                link(dve.scalar_tensor_tensor(out=slot_f, in0=first_f, scalar=2.0, in1=q_f,
                                              op0=ALU.mult, op1=ALU.add))
                ts(m_f, iota_f[0:NB, 0:SLOTS], slot_f, None, ALU.is_equal).then_inc(idx_dve, 1)

            def index_4():
                dve.wait_ge(idx_pe, 4)
                link(dve.tensor_copy(rows_f[:, 0:T_LAST], rows_ps))
                link(ts(rows_f[:, T_LAST:T_END], rows_f[:, T_START + 1:T_USED], 1.0, None, ALU.subtract))
                link(ts(rows_f[:, T_ADAPTER:T_START], rows_f[:, T_ADAPTER:T_START], float(NW), None, ALU.add))
                link(ts(slot_iota, iota_f[0:1, 0:SLOTS], float(DUMMY), None, ALU.add))
                link(ts(m_f[0:1, :], fill_ps, -1.0, 1.0, ALU.mult, ALU.add))
                link(tt(slot_iota, slot_iota, m_f[0:1, :], ALU.mult))
                link(tt(rows_f[:, T_STORE:T_ADAPTER], rows_f[:, T_LOAD:T_STORE], slot_iota, ALU.add))
                dve.tensor_copy(table[0:1, :], rows_f).then_inc(table_ready, 1)

            def second_layer_constants():
                for m in range(GT):
                    link(ts(desc1[:, m, :], iota_f[:, 0:E1], -1.0, float(E1), ALU.mult, ALU.add))
                link(ts(q_f[0:2 * E1, :], part_f[0:2 * E1, :], float(E1), float(E1), ALU.is_ge, ALU.mult))
                link(tt(q_f[0:2 * E1, :], part_f[0:2 * E1, :], q_f[0:2 * E1, :], ALU.subtract))
                link(ts(tmp_f[0:2 * E1, 0:E1], iota_f[0:2 * E1, 0:E1], q_f[0:2 * E1, :], None, ALU.is_equal))
                link(dve.tensor_copy(sel[:, :, :].rearrange("q j (h r) -> q (j h) r", r=R1),
                                     bcast(tmp_f[0:2 * E1, 0:E1], 2, R1)))
                tt(q_lo[:, :, :], q1raw[:, :, :], q_hi[:, :, :].bitcast(F32), ALU.subtract).then_inc(const_split, 1)

            def gates(link, n, desc, shift_sem, exp_sem, turn, eps):
                T = sm[:, :, :, 0:n]
                mx, k1, k2, m2, s, r, zz = (sv[:, i, :] for i in range(7))
                lg, sh, e, oh1, sh2, c, oh2, em, w = (T[:, i] for i in (2, 0, 1, 3, 4, 5, 6, 7, 8))
                link(dve.reduce_max(mx, lg, AX.X))
                tt(sh, lg, bcast(mx, 2, n), ALU.subtract).then_inc(shift_sem, 1)
                dve.wait_ge(shift_sem, turn)
                link(dve.scalar_tensor_tensor(out=c, in0=sh, scalar=0.0, in1=desc[:, :, :], op0=ALU.is_equal, op1=ALU.mult))
                link(dve.reduce_max(k1, c, AX.X))
                link(tt(oh1, desc[:, :, :], bcast(k1, 2, n), ALU.is_equal))
                link(dve.scalar_tensor_tensor(out=sh2, in0=oh1, scalar=-BIG, in1=sh, op0=ALU.mult, op1=ALU.add))
                link(dve.reduce_max(m2, sh2, AX.X))
                link(tt(c, sh2, bcast(m2, 2, n), ALU.is_equal))
                link(tt(c, c, desc[:, :, :], ALU.mult))
                link(dve.reduce_max(k2, c, AX.X))
                link(tt(oh2, desc[:, :, :], bcast(k2, 2, n), ALU.is_equal))
                link(tt(oh2, oh1, oh2, ALU.add))
                dve.wait_ge(exp_sem, turn)
                link(tt(em, e, oh2, ALU.mult))
                link(dve.reduce_sum(s, em, AX.X))
                if eps:
                    link(dve.reduce_sum(zz, e, AX.X))
                    link(dve.scalar_tensor_tensor(out=s, in0=zz, scalar=eps, in1=s, op0=ALU.mult, op1=ALU.add))
                link(dve.reciprocal(r, s))
                link(dve.scalar_tensor_tensor(out=w, in0=em, scalar=0.5, in1=bcast(r, 2, n), op0=ALU.mult, op1=ALU.mult))
                return w

            CH0 = 16

            def gates0(g):
                ln = Chain(dve, gate_chain, g * CH0)
                dve.wait_ge(yz_done, g + 1)
                ln(tt(sm[:, 2, :, 0:E0], yz_ps[:, :, 0:E0], bcast(rbias[:, :], 1, GT), ALU.add))
                w = gates(ln, E0, desc0, shift0, exp0, g + 1, None)
                assert not isinstance(g, int) or ln.value == (g + 1) * CH0
                for m in range(GT):
                    tt(hw0[:, m, :].rearrange("p (e r) -> p e r", e=E0),
                       yz_ps[:, m, E0:Z0].rearrange("p (e r) -> p e r", e=E0),
                       bcast(w[:, m, :], 2, R0), ALU.mult).then_inc(hw0_ready, 1)

            def hidden_low(g):
                dve.wait_ge(h0_hi_done, g + 1)
                tt(h0_lo[:, :], h0T_ps, h0_hi[:, :].bitcast(F32), ALU.subtract).then_inc(h0_lo_done, 1)

            def add_x(g, slot):
                dve.wait_ge(x1_out[slot % 2], (g - slot % 2) * 8 + 16)
                for q in range(4):
                    dve.wait_ge(o_done, 4 * g + q + 1)
                    ks = slice(2 * q, 2 * q + 2)
                    tt(x1g[slot % 2][:, :, ks, :].rearrange("p b i c -> p i b c"),
                       bank(3 + q).rearrange("p (i b c) -> p i b c", i=2, b=GB),
                       xg[slot][:, ks, :].rearrange("p i (b c) -> p i b c", b=GB), ALU.add).then_inc(x1_added, 1)

            def step0(g, slot):
                gates0(g + 1)
                add_x(g, slot)
                hidden_low(g + 1)

            index_0()
            for m in range(GT):
                link(ts(desc0[:, m, :], iota_f[:, 0:E0], -1.0, float(E0), ALU.mult, ALU.add))
            dve.wait_ge(const_split_hi, 1)
            tt(b0_lo[:, :], b0raw[:, :], b0_hi[:, :].bitcast(F32), ALU.subtract).then_inc(const_split, 1)
            gates0(0)
            hidden_low(0)
            for s, more in enumerate((index_1, index_2, index_3, index_4)):
                step0(s, s)
                more()
            dve.wait_ge(const_split_hi, 2)
            second_layer_constants()
            with dve.Fori(1, NG // RING - 1) as t:
                for s in range(RING):
                    step0(t * RING + s, s)
            for s in range(RING - 1):
                step0(NG - RING + s, s)
            add_x(NG - 1, RING - 1)

            def w_low(n, i):
                dve.wait_ge(w_hi_done, n * KC + i + 1)
                tt(w_lo[:, i, :], raw[:, i, :], w_hi[:, i, :].bitcast(F32), ALU.subtract).then_inc(w_lo_done, 1)

            def x_low(j, half):
                ks = slice(half * KC // 2, (half + 1) * KC // 2)
                dve.wait_ge(xp_hi_done, 2 * j + half + 1)
                tt(xp_lo[:, ks, :].rearrange("p i (b c) -> p b i c", b=2), xp_of(j, ks),
                   xp_hi[:, ks, :].bitcast(F32).rearrange("p i (b c) -> p b i c", b=2), ALU.subtract
                   ).then_inc(xp_lo_done, 1)

            def step(j, u_next=None):
                for i in range(KC):
                    if u_next is not None:
                        w_low(u_next, i)
                    if i == KC // 2 - 1:
                        x_low(j + 1, 0)
                x_low(j + 1, 1)
                dve.wait_ge(mm_done, KC * j + KC)
                dve.wait_ge(yp_out, 32 * j + 32)
                dve.tensor_copy(yp[:, 512:1024], psum[:, bass.ds(((j % 2) * 2 + 4) * 512, 512)]
                                ).then_inc(yp_dve, 1)

            x_low(0, 0)
            x_low(0, 1)
            for i in range(KC):
                dve.wait_ge(base_hi_done, i + 1)
                tt(base_lo[:, i, :], raw[:, i, :], base_hi[:, i, :].bitcast(F32), ALU.subtract
                   ).then_inc(base_lo_done, 1)
            dve.wait_ge(table_ready, 1)
            used = w_used(dve)
            with dve.Fori(0, used) as u:
                first = start_of(dve, u)
                last = last_of(dve, u)
                with dve.If(last > first):
                    with dve.Fori(first, last) as j:
                        step(j)
                with dve.Else():
                    dve.nop()
                step(last, u + 1)

            def y_low(g):
                for q in range(4):
                    dve.wait_ge(y_hi_done, 4 * g + q + 1)
                    tt(y_lo[:, 2 * q:2 * q + 2, :], bank(4 + q % 2).rearrange("p (i r) -> p i r", i=2),
                       y_hi[:, 2 * q:2 * q + 2, :].bitcast(F32), ALU.subtract).then_inc(y_lo_done, 1)

            CH1 = 19
            chain_b = NG * CH0

            def group1(g):
                ln = Chain(dve, gate_chain, chain_b + g * CH1)
                dve.wait_ge(lt_done, g + 1)
                ln(dve.tensor_copy(sm[:, 2, :, :], bank(7)[:, 0:GT * E1].rearrange("p (m e) -> p m e", m=GT)))
                w = gates(ln, E1, desc1, shift1, exp1, g + 1, 1e-6)
                ln(dve.tensor_copy(comb_r[:, :, :], w))
                assert not isinstance(g, int) or ln.value == chain_b + (g + 1) * CH1
                hi = comb_r[:, :, :].bitcast(F32)
                tt(comb[:, :, E1:2 * E1], w, hi, ALU.subtract).then_inc(comb_ready, 1)
                dve.tensor_copy(comb[:, :, 0:E1], hi).then_inc(comb_ready, 1)

                def low(j):
                    dve.wait_ge(hw_hi_done, KC * g + j + 1)
                    tt(hw_lo[:, j, :], hwt[j % 2][:, :], hw_hi[:, j, :].bitcast(F32), ALU.subtract
                       ).then_inc(hw_lo_done, 1)

                for j in range(KC):
                    dve.wait_ge(bc_done, KC * g + j + 1)
                    if j >= 2:
                        dve.wait_ge(hw_lo_done, KC * g + j - 1)
                    tt(hwt[j % 2][:, :], bank(4 + j % 2)[:, 0:GR], rh2[:, :], ALU.mult).then_inc(hwt_ready, 1)
                    if j > 0:
                        low(j - 1)
                low(KC - 1)

            def sums(g, q):
                for o in (2 * q, 2 * q + 1):
                    dve.wait_ge(acc_done, 4 * g + q + 1)
                    X = xr[:, :, o, :]
                    dve.scalar_tensor_tensor(out=X, in0=psum[:, o * GR:(o + 1) * GR].rearrange("p (b c) -> p b c", b=GB),
                                             scalar=bias[:, o:o + 1], in1=X, op0=ALU.add, op1=ALU.add
                                             ).then_inc(out_added, 1)

            y_low(0)
            with dve.Fori(0, NG - 1) as g:
                group1(g)
                dve.wait_ge(xr_in, 16 * g + 16)
                for q in range(4):
                    dve.wait_ge(y_hi_done, 4 * g + 4 + q + 1)
                    tt(y_lo[:, 2 * q:2 * q + 2, :], bank(4 + q % 2).rearrange("p (i r) -> p i r", i=2),
                       y_hi[:, 2 * q:2 * q + 2, :].bitcast(F32), ALU.subtract).then_inc(y_lo_done, 1)
                    sums(g, q)
            group1(NG - 1)
            dve.wait_ge(xr_in, 16 * NG)
            for q in range(4):
                sums(NG - 1, q)

        @block.tensor
        def _(pe):
            mm = pe.matmul

            def index_sums(n):
                pe.wait_ge(idx_dve, n)
                if n == 1:
                    last = mm(prefix_ps, before_f, hot_f, start=True, stop=True)
                elif n == 2:
                    mm(npb_ps, ones_f, hot_even_f, start=True, stop=True)
                    last = mm(npc_ps, hot_f, even_f, start=True, stop=True)
                elif n == 3:
                    mm(pos_ps, hotT_f, pos_f, start=True, stop=True)
                    last = mm(start_ps, npw_f, g_f, start=True, stop=True)
                else:
                    mm(rows_ps[:, T_LOAD:T_STORE], part_f[0:NB, :], m_f, start=True, stop=True)
                    mm(rows_ps[:, T_STORE:T_ADAPTER], part_f[0:NB, :], m_f, start=True, stop=True)
                    mm(rows_ps[:, T_ADAPTER:T_START], part16_f, r_f, start=True, stop=True)
                    mm(rows_ps[:, T_START:T_USED], np_f, g_f, start=True, stop=True)
                    mm(rows_ps[:, T_USED:T_LAST], used_f, ones_f[0:NW, 0:1], start=True, stop=True)
                    last = mm(fill_ps, ones_f[:, 0:1], m_f, start=True, stop=True)
                last.then_inc(idx_pe, 1)

            def split_product(out, a_hi, a_lo, b_hi, b_lo, start, stop):
                mm(out, a_hi, b_hi, start=start, stop=False, skip_group_check=True)
                mm(out, a_hi, b_lo, start=False, stop=False, skip_group_check=True)
                return mm(out, a_lo, b_hi, start=False, stop=stop, skip_group_check=True)

            def z_of(g, slot):
                pe.wait_ge(xg_in[slot], (g + RING - slot) * (16 // RING))
                if not (isinstance(g, int) and g == 0):
                    pe.wait_ge(z_copied, g)
                for m in range(GT):
                    for i in range(KC):
                        last = mm(z_ps[:, m, :], xg[slot][:, i, m * P:(m + 1) * P], p0[:, i, :],
                                  start=i == 0, stop=i == KC - 1)
                last.then_inc(z_done, 1)

            def y_of(g, slot):
                pe.wait_ge(z_copied, g + 1)
                pe.wait_ge(blk_ready, 4 * g + 4)
                if not (isinstance(g, int) and g == 0):
                    pe.wait_ge(hw0_ready, 2 * g)
                for m in range(GT):
                    last = mm(yz_ps[:, m, :], w0blk[slot % 2][:, m, :], zsb[:, m, :], start=True, stop=True)
                last.then_inc(yz_done, 1)

            def group0(g, slot, last_group=False):
                if not last_group:
                    z_of(g + 1, (slot + 1) % RING)
                pe.wait_ge(hw0_ready, 2 * g + 2)
                if not (isinstance(g, int) and g == 0):
                    pe.wait_ge(h0_lo_done, g)
                for m in range(GT):
                    last = pe.transpose(h0T_ps[:, m * P:(m + 1) * P], hw0[:, m, :], ident[:, :])
                last.then_inc(h0T_done, 1)
                if not last_group:
                    y_of(g + 1, slot + 1)
                pe.wait_ge(h0_lo_done, g + 1)
                for q in range(4):
                    if not (isinstance(g, int) and g == 0):
                        pe.wait_ge(x1_added, 4 * g + q - 3)
                    for i in (2 * q, 2 * q + 1):
                        o = bank(3 + q)[:, (i % 2) * GR:(i % 2 + 1) * GR]
                        last = split_product(o, b0_hi[:, i * P:(i + 1) * P], b0_lo[:, i * P:(i + 1) * P],
                                             h0_hi[:, :], h0_lo[:, :], i % 2 == 0, i % 2 == 1)
                    last.then_inc(o_done, 1)

            pe.wait_ge(p0_in, 16)
            z_of(0, 0)
            y_of(0, 0)
            pe.wait_ge(ident_done, 2)
            for s in range(RING):
                if s == 0:
                    pe.wait_ge(const_split, 1)
                group0(s, s)
                index_sums(s + 1)
            with pe.Fori(1, NG // RING - 1) as t:
                g0 = t * RING
                for s in range(RING):
                    group0(g0 + s, s)
            for s in range(RING):
                group0(NG - RING + s, s, last_group=s == RING - 1)
            pe.wait_ge(x1_added, 4 * NG)

            pe.wait_ge(table_ready, 1)
            used = w_used(pe)
            with pe.Fori(0, used) as u:
                first = start_of(pe, u)
                end = start_of(pe, u + 1)
                with pe.Fori(first, end) as j:
                    for i in range(KC):
                        if i % (KC // 2) == 0:
                            pe.wait_ge(xp_lo_done, 2 * j + i // (KC // 2) + 1)
                        pe.wait_ge(w_lo_done, u * KC + i + 1)
                        for h in range(2):
                            hs = slice(h * 512, (h + 1) * 512)
                            last = split_product(psum[:, bass.ds(((j % 2) * 2 + 3 + h) * 512, 512)],
                                                 xp_hi[:, i, :], xp_lo[:, i, :],
                                                 w_hi[:, i, hs], w_lo[:, i, hs], i == 0, i == KC - 1)
                        last.then_inc(mm_done, 1)

            def transposes(g, q):
                if q == 0:
                    pe.wait_ge(yn_in, 16 * g + 16)
                if not (isinstance(g, int) and g == 0 and q < 2):
                    pe.wait_ge(y_lo_done, 4 * g + q - 1)
                for i in range(2):
                    for m in range(GT):
                        last = pe.transpose(bank(4 + q % 2)[:, (i * GT + m) * P:(i * GT + m + 1) * P],
                                            yn[:, m, (2 * q + i) * P:(2 * q + i + 1) * P], ident[:, :])
                last.then_inc(yT_done, 1)

            def rh_of(g):
                pe.wait_ge(y_lo_done, 4 * g + 4)
                for i in range(KC):
                    last = split_product(bank(6)[0:Z1, 0:GR], q_hi[:, i, :], q_lo[:, i, :],
                                         y_hi[:, i, :], y_lo[:, i, :], i == 0, i == KC - 1)
                last.then_inc(rh_done, 1)

            def acc(o):
                return psum[:, o * GR:(o + 1) * GR]

            def spread_gates(g, j):
                if j == 0:
                    pe.wait_ge(combT_ready, g + 1)
                if j >= 2:
                    pe.wait_ge(hwt_ready, KC * g + j - 1)
                mm(bank(4 + j % 2)[:, 0:GR], sel[:, j, :], combT[:, :], start=True, stop=True).then_inc(bc_done, 1)

            def group1(g, last_group=False):
                for o in range(KC):
                    if o % 2 == 0 and not (isinstance(g, int) and g == 0):
                        pe.wait_ge(out_added, KC * g - KC + o + 2)
                    for k in range(KC):
                        ws = slice(o * P, (o + 1) * P)
                        if o == 0 and k == KC - 1:
                            pe.wait_ge(rh_copied, 3 * g + 3)
                        last = split_product(acc(o), base_hi[:, k, ws], base_lo[:, k, ws],
                                             y_hi[:, k, :], y_lo[:, k, :], k == 0 and o % 2 == 0, False)
                        if o >= KC // 2 and k % (KC // 2) == 0:
                            spread_gates(g, 2 * (o - KC // 2) + k // (KC // 2))
                    if o == 0:
                        for m in range(GT):
                            t = pe.transpose(bank(7)[:, m * E1:(m + 1) * E1], lgT[:, m * P:(m + 1) * P],
                                             ident[0:E1, 0:E1])
                        t.then_inc(lt_done, 1)
                    if o == 3:
                        pe.wait_ge(comb_ready, 2 * g + 2)
                        for m in range(GT):
                            t = pe.transpose(bank(7)[0:2 * E1, m * P:(m + 1) * P], comb[:, m, :], ident[:, :])
                        t.then_inc(ct_done, 1)
                last.then_inc(base_done, 1)
                for o in range(KC):
                    for k in range(KC):
                        ws = slice(o * P, (o + 1) * P)
                        if o == 0:
                            pe.wait_ge(hw_lo_done, KC * g + k + 1)
                        last = split_product(acc(o), w_hi[:, k, ws], w_lo[:, k, ws],
                                             hw_hi[:, k, :], hw_lo[:, k, :], False, k == KC - 1)
                    if o % 2 == 1:
                        last.then_inc(acc_done, 1)
                    elif not last_group:
                        transposes(g + 1, o // 2)
                if not last_group:
                    rh_of(g + 1)

            total = start_of(pe, used)
            pe.wait_ge(yp_act, total)
            pe.wait_ge(yp_dve, total)
            pe.wait_ge(base_lo_done, KC)
            pe.wait_ge(const_split, 2)
            for q in range(4):
                transposes(0, q)
            rh_of(0)
            pe.wait_ge(w_lo_done, used * KC + KC)
            group1(0)
            with pe.Fori(1, NG - 1) as g:
                group1(g)
            group1(NG - 1, last_group=True)


def kernel(**inputs):
    import numpy as np
    import concourse.bacc as bacc
    from concourse.bass_utils import run_bass_kernel_spmd

    a = {k: np.asarray(v) for k, v in inputs.items()}
    chunked = lambda m: m.reshape(KC, P, -1).transpose(1, 0, 2)
    experts_b = a["L1_ffn_B"].transpose(0, 2, 1).reshape(1, E1 * R1, D)
    adapters = a["L1_cond_weight"].transpose(0, 2, 1)
    arrays = {
        "xT": a["x"].reshape(NG, GR, KC, P).transpose(0, 3, 2, 1),
        "id0": a["itok_B_0_15"],
        "id1": a["itok_B_1_14"],
        "w0": a["L0_cond_weights"].transpose(1, 0, 2).reshape(C, NW * C),
        "p0T": chunked(np.concatenate([a["L0_ffn_router_w"], a["L0_ffn_A"].reshape(E0 * R0, D)]).T),
        "rb0": a["L0_ffn_router_b"],
        "b0T": a["L0_ffn_Bm"].transpose(0, 2, 1).reshape(E0 * R0, D),
        "w1T": np.concatenate([adapters, experts_b]).reshape(NW + 1, KC, P, D),
        "baseT": a["L1_ffn_base_w"].T.reshape(KC, P, D),
        "q1T": chunked(np.concatenate([a["L1_ffn_A"], a["L1_ffn_router_w"]]).T),
        "bias1": a["L1_ffn_base_b"].reshape(KC, P).T,
    }
    nc = bacc.Bacc("TRN2", target_bir_lowering=False, num_devices=1)
    feeds, args = {}, []
    for name, array in arrays.items():
        array = np.ascontiguousarray(array)
        feeds[name] = array
        args.append(nc.dram_tensor(name, array.shape, mybir.dt.from_np(array.dtype), kind="ExternalInput").ap())
    out = nc.dram_tensor("out", (NB, P, KC * C), F32, kind="ExternalOutput").ap()
    build(nc, *args, out)
    got = run_bass_kernel_spmd(nc, [feeds], core_ids=[0]).results[0]["out"]
    return got.reshape(NB, P, KC, C).transpose(0, 3, 2, 1).reshape(NB, C, D)
```
